# Optimizing a Trainium2 kernel written in Bass

```python
import numpy as np
import jax
import jax.numpy as jnp

def _softmax(x, axis=-1):
    return jax.nn.softmax(x, axis=axis)

def _gelu(x):
    return jax.nn.gelu(x, approximate=True)

def _silu(x):
    return jax.nn.silu(x)

def _sigmoid(x):
    return jax.nn.sigmoid(x)

def _layernorm(x, axis=-1, eps=1e-05):
    m = jnp.mean(x, axis=axis, keepdims=True)
    v = jnp.var(x, axis=axis, keepdims=True)
    return (x - m) / jnp.sqrt(v + eps)

def _scatter_add(tgt, idx, src, axis=0):
    return tgt.at[idx].add(src)

def _segment_sum(src, seg, n):
    return jax.ops.segment_sum(src, seg, n)
kernel_name = 'mk_rec_standalone_d1_rec_r8_93072a'

def setup_inputs(seed: int=0):
    np.random.seed(seed)
    _w = jnp.asarray

    def _rec_inputs():
        import jax
        import jax.numpy as jnp
        _rk = jax.random.key(seed)
        r_us = jax.random.bernoulli(jax.random.fold_in(_rk, 1), 0.5044, (1024, 1)).astype(jnp.float32)
        r_them = jax.random.bernoulli(jax.random.fold_in(_rk, 2), 0.4956, (1024, 1)).astype(jnp.float32)
        r_w_in = jax.random.bernoulli(jax.random.fold_in(_rk, 3), 0.0007304, (1024, 5128)).astype(jnp.float32)
        r_b_in = jax.random.bernoulli(jax.random.fold_in(_rk, 4), 0.0007336, (1024, 5128)).astype(jnp.float32)
        return (r_us, r_them, r_w_in, r_b_in)
    r_us, r_them, r_w_in, r_b_in = _rec_inputs()

    def _L0_rec_setup():
        import jax, jax.numpy as jnp
        import numpy as np
        INPUTS = 5128
        L1, L2, L3 = (128, 32, 32)
        B = 512
        ACTIVE_P = 30.0 / INPUTS
        key = jax.random.key(seed)
        ks = jax.random.split(key, 10)
        us = jax.random.randint(ks[0], (B, 1), 0, 2).astype(jnp.float32)
        them = 1.0 - us

        def sparse_feats(k):
            k1, k2 = jax.random.split(k)
            mask = jax.random.bernoulli(k1, ACTIVE_P, (B, INPUTS))
            return mask.astype(jnp.float32)
        w_in = sparse_feats(ks[1])
        b_in = sparse_feats(ks[2])
        s = 0.02
        W_ft = jax.random.normal(ks[3], (INPUTS, L1), dtype=jnp.float32) * s
        b_ft = jax.random.normal(ks[4], (L1,), dtype=jnp.float32) * s
        W1 = jax.random.normal(ks[5], (2 * L1, L2), dtype=jnp.float32) * s
        b1 = jax.random.normal(ks[6], (L2,), dtype=jnp.float32) * s
        W2 = jax.random.normal(ks[7], (L2, L3), dtype=jnp.float32) * s
        b2 = jax.random.normal(ks[8], (L3,), dtype=jnp.float32) * s
        Wo = jax.random.normal(ks[9], (L3, 1), dtype=jnp.float32) * s
        bo = jnp.zeros((1,), dtype=jnp.float32)
        return {'us': us, 'them': them, 'w_in': w_in, 'b_in': b_in, 'W_ft': W_ft, 'b_ft': b_ft, 'W1': W1, 'b1': b1, 'W2': W2, 'b2': b2, 'Wo': Wo, 'bo': bo}
    _L0_rec_all = _L0_rec_setup()
    _L0_rec_in = {k: v for k, v in _L0_rec_all.items() if k in ('W_ft', 'b_ft', 'W1', 'b1', 'W2', 'b2', 'Wo', 'bo')}
    del _L0_rec_all
    return {'r_us': r_us, 'r_them': r_them, 'r_w_in': r_w_in, 'r_b_in': r_b_in, 'L0_rec_W_ft': _L0_rec_in['W_ft'], 'L0_rec_b_ft': _L0_rec_in['b_ft'], 'L0_rec_W1': _L0_rec_in['W1'], 'L0_rec_b1': _L0_rec_in['b1'], 'L0_rec_W2': _L0_rec_in['W2'], 'L0_rec_b2': _L0_rec_in['b2'], 'L0_rec_Wo': _L0_rec_in['Wo'], 'L0_rec_bo': _L0_rec_in['bo']}

def reference(r_us, r_them, r_w_in, r_b_in, L0_rec_W_ft, L0_rec_b_ft, L0_rec_W1, L0_rec_b1, L0_rec_W2, L0_rec_b2, L0_rec_Wo, L0_rec_bo):
    import jax
    import jax.numpy as jnp

    def _L0_rec_ref(us, them, w_in, b_in, W_ft, b_ft, W1, b1, W2, b2, Wo, bo):
        import jax, jax.numpy as jnp
        import numpy as np
        INPUTS = 5128
        L1, L2, L3 = (128, 32, 32)
        B = 512
        ACTIVE_P = 30.0 / INPUTS
        w = w_in @ W_ft + b_ft
        b = b_in @ W_ft + b_ft
        l0 = us * jnp.concatenate([w, b], axis=1) + them * jnp.concatenate([b, w], axis=1)
        l0 = jnp.clip(l0, 0.0, 1.0)
        l1 = jnp.clip(l0 @ W1 + b1, 0.0, 1.0)
        l2 = jnp.clip(l1 @ W2 + b2, 0.0, 1.0)
        return l2 @ Wo + bo
    y = _L0_rec_ref(r_us, r_them, r_w_in, r_b_in, L0_rec_W_ft, L0_rec_b_ft, L0_rec_W1, L0_rec_b1, L0_rec_W2, L0_rec_b2, L0_rec_Wo, L0_rec_bo)
    return y

_drawn_inputs = setup_inputs


def setup_inputs(seed=0):
    import zlib

    import numpy as np

    out = dict(_drawn_inputs(seed))
    spreads = {}
    factors = {}
    for name, (base, spread) in spreads.items():
        noise = np.random.default_rng([zlib.crc32(name.encode()), seed]).standard_normal(out[name].shape)
        drawn = base * np.exp(spread * noise) if base else spread * noise
        out[name] = jnp.asarray(drawn.astype(out[name].dtype))
    for name, factor in factors.items():
        out[name] = (out[name] * factor).astype(out[name].dtype)
    return out
```

```python
from contextlib import ExitStack

import concourse.bass as bass
from concourse import mybir

F32 = mybir.dt.float32
ALU = mybir.AluOpType

P = 128
ROWS = 1024
FEATS = 5128
L1, L2, L3 = 128, 32, 32
GROUPS = 4
GR = ROWS // GROUPS
GC = 2 * GR
T = 4
CHUNKS = FEATS // (P * T)
REM = FEATS - CHUNKS * T * P


def build(nc, x_main, x_rem, w_main, w_rem, b_ft, us, them, W1, b1, W2, b2, Wo, bo, out):
    with ExitStack() as ctx:
        def sb(name, shape, dt=F32):
            return ctx.enter_context(nc.sbuf_tensor(name, shape, dt))

        def sem(name):
            return ctx.enter_context(nc.semaphore(name))

        x_ring = sb("x_ring", [P, CHUNKS, T, GC])
        w_sb = sb("w_sb", [P, CHUNKS, T, L1])
        xr_sb = sb("xr_sb", [32, GROUPS, GC])
        wr_sb = sb("wr_sb", [32, L1])
        ut_row = sb("ut_row", [1, 2, ROWS])
        ones_row = sb("ones_row", [1, GR])
        ut = sb("ut", [P, 2, ROWS])
        w1_sb = sb("w1_sb", [P, 2, L2])
        b1_sb = sb("b1_sb", [1, L2])
        w2_sb = sb("w2_sb", [P, L3])
        wo_sb = sb("wo_sb", [P, 1])
        by_us = sb("by_us", [P, 2, GR])
        by_them = sb("by_them", [P, 2, GR])
        mixed = sb("mixed", [P, 2, GR])
        l0 = sb("l0", [P, 2, GR])
        l1 = sb("l1", [P, GR])
        l2 = sb("l2", [P, GR])
        y_sb = sb("y_sb", [1, ROWS])

        ft = ctx.enter_context(nc.psum_tensor("ft", [P, GROUPS, GC], F32))
        bc = ctx.enter_context(nc.psum_tensor("bc", [P, 4, 512], F32))
        h1, h2, hy = bc[0:L2, 0, 0:GR], bc[0:L3, 1, 0:GR], bc[0:1, 2, 0:GR]

        x_landed = [sem(f"x_landed{c}") for c in range(CHUNKS)]
        slot_used = [sem(f"slot_used{c}") for c in range(CHUNKS)]
        w_landed = [sem(f"w_landed{c}") for c in range(CHUNKS)]
        zero_filled = sem("zero_filled")
        rem_landed = sem("rem_landed")
        ut_landed = sem("ut_landed")
        head_landed = sem("head_landed")
        ones_set = sem("ones_set")
        ut_spread = sem("ut_spread")
        ut_copied = sem("ut_copied")
        ft_done = sem("ft_done")
        mix_step = sem("mix_step")
        l0_ready = sem("l0_ready")
        h1_done = sem("h1_done")
        l1_ready = sem("l1_ready")
        h2_done = sem("h2_done")
        l2_ready = sem("l2_ready")
        hy_done = sem("hy_done")
        y_ready = sem("y_ready")
        out_stored = sem("out_stored")

        block = ctx.enter_context(nc.Block())

        @block.sync
        def _(sp):
            for c in range(CHUNKS):
                sp.dma_start(w_sb[:, c], w_main[c]).then_inc(w_landed[c], 16)
                sp.dma_start(x_ring[:, c], x_main[0, c]).then_inc(x_landed[c], 16)
            with sp.Fori(1, GROUPS) as g:
                for c in range(CHUNKS):
                    sp.wait_ge(slot_used[c], g)
                    sp.dma_start(x_ring[:, c], x_main[g, c]).then_inc(x_landed[c], 16)
            sp.wait_ge(y_ready, GROUPS)
            sp.dma_start(out, y_sb[:, :]).then_inc(out_stored, 16)
            sp.wait_ge(out_stored, 16)

        @block.gpsimd
        def _(pool):
            nc.gpsimd.memset(xr_sb[:], 1.0).then_inc(zero_filled, 1)
            nc.gpsimd.memset(wr_sb[:], 0.0).then_inc(zero_filled, 1)
            nc.gpsimd.memset(w2_sb[:], 0.0).then_inc(zero_filled, 1)
            nc.gpsimd.memset(wo_sb[:], 0.0).then_inc(zero_filled, 1)

        @block.scalar
        def _(act):
            act.dma_start(ut_row[:, 0], us).then_inc(ut_landed, 16)
            act.dma_start(ut_row[:, 1], them).then_inc(ut_landed, 16)
            act.wait_ge(zero_filled, 4)
            act.dma_start(xr_sb[0:REM, :, :], x_rem).then_inc(rem_landed, 16)
            act.dma_start(wr_sb[0:REM, :], w_rem).then_inc(rem_landed, 16)
            act.dma_start(wr_sb[REM:REM + 1, :], b_ft).then_inc(rem_landed, 16)
            for dst, src in ((w1_sb[:], W1), (b1_sb[:], b1), (w2_sb[0:L2], W2), (w2_sb[L2:L2 + 1], b2),
                             (wo_sb[0:L3], Wo), (wo_sb[L3:L3 + 1], bo)):
                act.dma_start(dst, src).then_inc(head_landed, 16)
            for h in range(4):
                act.wait_ge(ut_spread, h + 1)
                nc.scalar.copy(ut[:, h // 2, 512 * (h % 2):512 * (h % 2) + 512], bc[:, h]).then_inc(ut_copied, 1)

        @block.tensor
        def _(pe):
            def transform(g, first):
                for c in range(CHUNKS):
                    if first:
                        pe.wait_ge(w_landed[c], 16)
                    pe.wait_ge(x_landed[c], 16 * (g + 1))
                    for t in range(T):
                        mm = nc.tensor.matmul(ft[:, g], w_sb[:, c, t], x_ring[:, c, t],
                                              start=(c == 0 and t == 0), stop=False)
                    mm.then_inc(slot_used[c], 1)
                    if not first:
                        if c == 2:
                            head_1(g - 1)
                        if c == 3:
                            head_2(g - 1)
                        if c == 4:
                            head_y(g - 1)
                if first:
                    pe.wait_ge(rem_landed, 48)
                nc.tensor.matmul(ft[:, g], wr_sb[:, :], xr_sb[:, g], start=False, stop=True).then_inc(ft_done, 1)

            def head_1(g):
                nc.tensor.matmul(h1, b1_sb[:, :], ones_row[:, :], start=True, stop=False)
                pe.wait_ge(l0_ready, g + 1)
                nc.tensor.matmul(h1, w1_sb[:, 0], l0[:, 0], start=False, stop=False)
                nc.tensor.matmul(h1, w1_sb[:, 1], l0[:, 1], start=False, stop=True).then_inc(h1_done, 1)

            def head_2(g):
                pe.wait_ge(l1_ready, g + 1)
                nc.tensor.matmul(h2, w2_sb[:, :], l1[:, :], start=True, stop=True).then_inc(h2_done, 1)

            def head_y(g):
                pe.wait_ge(l2_ready, g + 1)
                nc.tensor.matmul(hy, wo_sb[:, :], l2[:, :], start=True, stop=True).then_inc(hy_done, 1)

            pe.wait_ge(ones_set, 1)
            pe.wait_ge(ut_landed, 32)
            for h in range(4):
                nc.tensor.matmul(bc[:, h], ones_row[:, 0:P], ut_row[:, h // 2, 512 * (h % 2):512 * (h % 2) + 512],
                                 start=True, stop=True).then_inc(ut_spread, 1)
            transform(0, True)
            pe.wait_ge(head_landed, 96)
            pe.wait_ge(ut_copied, 4)
            with pe.Fori(1, GROUPS) as g:
                transform(g, False)
            head_1(GROUPS - 1)
            head_2(GROUPS - 1)
            head_y(GROUPS - 1)

        @block.vector
        def _(dve):
            nc.vector.memset(ones_row[:], 1.0).then_inc(ones_set, 1)
            nc.vector.memset(l1[:], 1.0).then_inc(ones_set, 1)
            nc.vector.memset(l2[:], 1.0).then_inc(ones_set, 1)
            dve.wait_ge(ones_set, 3)
            dve.wait_ge(ut_copied, 4)
            with dve.Fori(0, GROUPS) as g:
                u = ut[:, 0:1, bass.ts(g, GR)].to_broadcast([P, 2, GR])
                t = ut[:, 1:2, bass.ts(g, GR)].to_broadcast([P, 2, GR])
                acc = ft[:, g].rearrange("p (s r) -> p s r", s=2)
                dve.wait_ge(ft_done, g + 1)
                nc.vector.tensor_tensor(by_us[:], acc, u, ALU.mult).then_inc(mix_step, 1)
                nc.vector.tensor_tensor(by_them[:], acc, t, ALU.mult).then_inc(mix_step, 1)
                dve.wait_ge(mix_step, 4 * g + 2)
                nc.vector.tensor_tensor(mixed[:, 0], by_us[:, 0], by_them[:, 1], ALU.add).then_inc(mix_step, 1)
                nc.vector.tensor_tensor(mixed[:, 1], by_us[:, 1], by_them[:, 0], ALU.add).then_inc(mix_step, 1)
                dve.wait_ge(mix_step, 4 * g + 4)
                nc.vector.tensor_scalar(l0[:], mixed[:], 0.0, 1.0, ALU.max, ALU.min).then_inc(l0_ready, 1)
                dve.wait_ge(h1_done, g + 1)
                nc.vector.tensor_scalar(l1[0:L2, :], h1, 0.0, 1.0, ALU.max, ALU.min).then_inc(l1_ready, 1)
                dve.wait_ge(h2_done, g + 1)
                nc.vector.tensor_scalar(l2[0:L3, :], h2, 0.0, 1.0, ALU.max, ALU.min).then_inc(l2_ready, 1)
                dve.wait_ge(hy_done, g + 1)
                nc.vector.tensor_copy(y_sb[:, bass.ts(g, GR)], hy).then_inc(y_ready, 1)


def kernel(r_us, r_them, r_w_in, r_b_in, L0_rec_W_ft, L0_rec_b_ft, L0_rec_W1, L0_rec_b1, L0_rec_W2, L0_rec_b2,
           L0_rec_Wo, L0_rec_bo):
    import numpy as np
    import concourse.bacc as bacc
    from concourse.bass_utils import run_bass_kernel_spmd

    flat = CHUNKS * T * P
    both = np.stack([np.asarray(r_w_in), np.asarray(r_b_in)])
    w_ft = np.asarray(L0_rec_W_ft)
    main = both[:, :, :flat].reshape(2, GROUPS, GR, CHUNKS, T, P).transpose(1, 3, 5, 4, 0, 2)
    rem = both[:, :, flat:].reshape(2, GROUPS, GR, REM).transpose(3, 1, 0, 2)
    arrays = {
        "x_main": main.reshape(GROUPS, CHUNKS, P, T, GC),
        "x_rem": rem.reshape(REM, GROUPS, GC),
        "w_main": w_ft[:flat].reshape(CHUNKS, T, P, L1).transpose(0, 2, 1, 3),
        "w_rem": w_ft[flat:],
        "b_ft": np.asarray(L0_rec_b_ft).reshape(1, L1),
        "us": np.asarray(r_us).reshape(1, ROWS),
        "them": np.asarray(r_them).reshape(1, ROWS),
        "W1": np.asarray(L0_rec_W1).reshape(2, L1, L2).transpose(1, 0, 2),
        "b1": np.asarray(L0_rec_b1).reshape(1, L2),
        "W2": np.asarray(L0_rec_W2),
        "b2": np.asarray(L0_rec_b2).reshape(1, L3),
        "Wo": np.asarray(L0_rec_Wo),
        "bo": np.asarray(L0_rec_bo).reshape(1, 1),
    }
    arrays = {name: np.ascontiguousarray(a) for name, a in arrays.items()}
    nc = bacc.Bacc("TRN2", target_bir_lowering=False, num_devices=1)
    args = [nc.dram_tensor(name, a.shape, mybir.dt.from_np(a.dtype), kind="ExternalInput").ap()
            for name, a in arrays.items()]
    out = nc.dram_tensor("out", (1, ROWS), F32, kind="ExternalOutput").ap()
    build(nc, *args, out)
    got = run_bass_kernel_spmd(nc, [arrays], core_ids=[0]).results[0]["out"]
    return got.reshape(ROWS, 1)
```

```python
from contextlib import ExitStack

import concourse.bass as bass
from concourse import mybir

F32 = mybir.dt.float32
BF16 = mybir.dt.bfloat16
U16 = mybir.dt.uint16
I32 = mybir.dt.int32
ACT = mybir.ActivationFunctionType
AX_X = mybir.AxisListType.X
ALU = mybir.AluOpType

P = 128
ROWS = 1024
FEATS = 5128
L1, L2, L3 = 128, 32, 32
GROUPS = 4
GR = ROWS // GROUPS
GC = 2 * GR
T = 4
CHUNKS = FEATS // (P * T)
REM = FEATS - CHUNKS * T * P


PART = 32
PARTS = 3
MAX_PASSES = 2 * GROUPS


def upper(ap):
    return ap.bitcast(BF16)[..., 1::2]


def lower(ap):
    return ap.bitcast(U16)[..., 0::2]


def build(nc, x_main, x_rem, w_main, w_rem, b_ft, us, them, W1, b1, W2, b2, Wo, bo, out):
    with ExitStack() as ctx:
        def sb(name, shape, dt=F32):
            return ctx.enter_context(nc.sbuf_tensor(name, shape, dt))

        def sem(name):
            return ctx.enter_context(nc.semaphore(name))

        x_ring = sb("x_ring", [P, CHUNKS, T, GC])
        w_sb = sb("w_sb", [P, CHUNKS, T, L1])
        w_rest = sb("w_rest", [P, CHUNKS, T, L1])
        w_low = sb("w_low", [P, CHUNKS, T, L1], BF16)
        xr_sb = sb("xr_sb", [PARTS * PART, GROUPS, GC])
        wr_sb = sb("wr_sb", [PARTS * PART, L1])
        wr_rest = sb("wr_rest", [PARTS * PART, L1])
        wr_parts = sb("wr_parts", [PARTS * PART, L1], BF16)
        low_sums = sb("low_sums", [P, GROUPS * CHUNKS + 1])
        low_copy = sb("low_copy", [P, 2, T, GC], BF16)
        low_max = sb("low_max", [P, 1])
        ones_col = sb("ones_col", [P, 1])
        redo = sb("redo", [1, 1], I32)
        ut_row = sb("ut_row", [1, 2, ROWS])
        ones_row = sb("ones_row", [1, GR])
        ut = sb("ut", [P, 2, ROWS])
        w1_sb = sb("w1_sb", [P, 2, L2])
        b1_sb = sb("b1_sb", [1, L2])
        w2_sb = sb("w2_sb", [P, L3])
        wo_sb = sb("wo_sb", [P, 1])
        by_us = sb("by_us", [P, 2, GR])
        by_them = sb("by_them", [P, 2, GR])
        mixed = sb("mixed", [P, 2, GR])
        l0 = sb("l0", [P, 2, GR])
        l1 = sb("l1", [P, GR])
        l2 = sb("l2", [P, GR])
        y_sb = sb("y_sb", [1, ROWS])

        ft = ctx.enter_context(nc.psum_tensor("ft", [P, GROUPS, GC], F32))
        bc = ctx.enter_context(nc.psum_tensor("bc", [P, 4, 512], F32))
        h1, h2, hy = bc[0:L2, 0, 0:GR], bc[0:L3, 1, 0:GR], bc[0:1, 2, 0:GR]
        low_total = bc[0:1, 3, 0:1]

        x_landed = [sem(f"x_landed{c}") for c in range(CHUNKS)]
        slot_used = [sem(f"slot_used{c}") for c in range(CHUNKS)]
        w_landed = [sem(f"w_landed{c}") for c in range(CHUNKS)]
        x_checked = [sem(f"x_checked{c}") for c in range(CHUNKS)]
        w_rested = sem("w_rested")
        w_split = sem("w_split")
        wr_step = sem("wr_step")
        zero_filled = sem("zero_filled")
        rem_landed = sem("rem_landed")
        ut_landed = sem("ut_landed")
        head_landed = sem("head_landed")
        ones_set = sem("ones_set")
        ut_spread = sem("ut_spread")
        ut_copied = sem("ut_copied")
        ft_done = sem("ft_done")
        mix_step = sem("mix_step")
        l0_ready = sem("l0_ready")
        h1_done = sem("h1_done")
        l1_ready = sem("l1_ready")
        h2_done = sem("h2_done")
        l2_ready = sem("l2_ready")
        hy_done = sem("hy_done")
        y_ready = sem("y_ready")
        out_stored = sem("out_stored")
        rem_checked = sem("rem_checked")
        low_maxed = sem("low_maxed")
        low_totalled = sem("low_totalled")
        redo_known = sem("redo_known")

        block = ctx.enter_context(nc.Block())

        @block.sync
        def _(sp):
            for c in range(CHUNKS):
                sp.dma_start(w_sb[:, c], w_main[c]).then_inc(w_landed[c], 16)
                sp.dma_start(x_ring[:, c], x_main[0, c]).then_inc(x_landed[c], 16)
            with sp.Fori(1, GROUPS) as g:
                for c in range(CHUNKS):
                    sp.wait_ge(slot_used[c], g)
                    sp.wait_ge(x_checked[c], g)
                    sp.dma_start(x_ring[:, c], x_main[g, c]).then_inc(x_landed[c], 16)
            sp.wait_ge(y_ready, GROUPS)
            sp.dma_start(out, y_sb[:, :]).then_inc(out_stored, 16)
            sp.wait_ge(out_stored, 16)
            sp.wait_ge(redo_known, 1)
            with sp.If(sp.value_load(redo[:, :], min_val=0, max_val=1) != 0):
                with sp.Fori(GROUPS, MAX_PASSES) as r:
                    for c in range(CHUNKS):
                        sp.wait_ge(slot_used[c], r)
                        sp.dma_start(x_ring[:, c], x_main[r - GROUPS, c]).then_inc(x_landed[c], 16)
                sp.wait_ge(y_ready, MAX_PASSES)
                sp.dma_start(out, y_sb[:, :]).then_inc(out_stored, 16)
                sp.wait_ge(out_stored, 32)

        @block.gpsimd
        def _(pool):
            nc.gpsimd.memset(xr_sb[:], 1.0).then_inc(zero_filled, 1)
            nc.gpsimd.memset(wr_sb[:], 0.0).then_inc(zero_filled, 1)
            nc.gpsimd.memset(w2_sb[:], 0.0).then_inc(zero_filled, 1)
            nc.gpsimd.memset(wo_sb[:], 0.0).then_inc(zero_filled, 1)

        @block.scalar
        def _(act):
            act.dma_start(ut_row[:, 0], us).then_inc(ut_landed, 16)
            act.dma_start(ut_row[:, 1], them).then_inc(ut_landed, 16)
            act.wait_ge(zero_filled, 4)
            for k in range(0, PARTS * PART, PART):
                act.dma_start(xr_sb[k:k + REM, :, :], x_rem).then_inc(rem_landed, 16)
                act.dma_start(wr_sb[k:k + REM, :], w_rem).then_inc(rem_landed, 16)
                act.dma_start(wr_sb[k + REM:k + REM + 1, :], b_ft).then_inc(rem_landed, 16)
            for dst, src in ((w1_sb[:], W1), (b1_sb[:], b1), (w2_sb[0:L2], W2), (w2_sb[L2:L2 + 1], b2),
                             (wo_sb[0:L3], Wo), (wo_sb[L3:L3 + 1], bo)):
                act.dma_start(dst, src).then_inc(head_landed, 16)
            for h in range(4):
                act.wait_ge(ut_spread, h + 1)
                nc.scalar.copy(ut[:, h // 2, 512 * (h % 2):512 * (h % 2) + 512], bc[:, h]).then_inc(ut_copied, 1)

            def sum_low(g, c, first):
                act.wait_ge(x_landed[c], 16 * (g + 1))
                if c >= 2:
                    act.wait_ge(x_checked[c - 2], g + 1)
                elif not first:
                    act.wait_ge(x_checked[c - 2], g)
                nc.scalar.activation(low_copy[:, c % 2], lower(x_ring[:, c]), ACT.Copy,
                                     accum_out=low_sums[:, bass.ds(g * CHUNKS + c, 1)]).then_inc(x_checked[c], 1)

            for c in range(CHUNKS):
                sum_low(0, c, True)
            with act.Fori(1, GROUPS) as g:
                for c in range(CHUNKS):
                    sum_low(g, c, False)
            act.wait_ge(rem_landed, 16 * 3 * PARTS)
            act.wait_ge(ones_set, 4)
            act.wait_ge(x_checked[CHUNKS - 2], GROUPS)
            nc.scalar.activation(low_copy[0:REM, 0], lower(xr_sb[0:REM]), ACT.Copy,
                                 accum_out=low_sums[0:REM, GROUPS * CHUNKS:]).then_inc(rem_checked, 1)

        @block.tensor
        def _(pe):
            def transform(g, first):
                for c in range(CHUNKS):
                    if first:
                        pe.wait_ge(w_landed[c], 16)
                    pe.wait_ge(x_landed[c], 16 * (g + 1))
                    for t in range(T):
                        nc.tensor.matmul(ft[:, g], upper(w_sb[:, c, t]), upper(x_ring[:, c, t]),
                                         start=(c == 0 and t == 0), stop=False)
                    if first:
                        pe.wait_ge(w_split, c + 1)
                    for t in range(T):
                        nc.tensor.matmul(ft[:, g], upper(w_rest[:, c, t]), upper(x_ring[:, c, t]),
                                         start=False, stop=False)
                        mm = nc.tensor.matmul(ft[:, g], w_low[:, c, t], upper(x_ring[:, c, t]),
                                              start=False, stop=False)
                    mm.then_inc(slot_used[c], 1)
                    if not first:
                        if c == 2:
                            head_1(g - 1)
                        if c == 3:
                            head_2(g - 1)
                        if c == 4:
                            head_y(g - 1)
                if first:
                    pe.wait_ge(rem_landed, 16 * 3 * PARTS)
                    pe.wait_ge(wr_step, 5)
                nc.tensor.matmul(ft[:, g], wr_parts[:, :], upper(xr_sb[:, g]), start=False,
                                 stop=True).then_inc(ft_done, 1)

            def transform_general(r, g):
                for c in range(CHUNKS):
                    pe.wait_ge(x_landed[c], 16 * (r + 1))
                    for t in range(T):
                        mm = nc.tensor.matmul(ft[:, g], w_sb[:, c, t], x_ring[:, c, t],
                                              start=(c == 0 and t == 0), stop=False)
                    mm.then_inc(slot_used[c], 1)
                nc.tensor.matmul(ft[:, g], wr_sb[0:PART, :], xr_sb[0:PART, g], start=False,
                                 stop=True).then_inc(ft_done, 1)

            def head_1(g):
                nc.tensor.matmul(h1, b1_sb[:, :], ones_row[:, :], start=True, stop=False)
                pe.wait_ge(l0_ready, g + 1)
                nc.tensor.matmul(h1, w1_sb[:, 0], l0[:, 0], start=False, stop=False)
                nc.tensor.matmul(h1, w1_sb[:, 1], l0[:, 1], start=False, stop=True).then_inc(h1_done, 1)

            def head_2(g):
                pe.wait_ge(l1_ready, g + 1)
                nc.tensor.matmul(h2, w2_sb[:, :], l1[:, :], start=True, stop=True).then_inc(h2_done, 1)

            def head_y(g):
                pe.wait_ge(l2_ready, g + 1)
                nc.tensor.matmul(hy, wo_sb[:, :], l2[:, :], start=True, stop=True).then_inc(hy_done, 1)

            pe.wait_ge(ones_set, 1)
            pe.wait_ge(ut_landed, 32)
            for h in range(4):
                nc.tensor.matmul(bc[:, h], ones_row[:, 0:P], ut_row[:, h // 2, 512 * (h % 2):512 * (h % 2) + 512],
                                 start=True, stop=True).then_inc(ut_spread, 1)
            transform(0, True)
            pe.wait_ge(head_landed, 96)
            pe.wait_ge(ut_copied, 4)
            with pe.Fori(1, GROUPS) as g:
                transform(g, False)
            head_1(GROUPS - 1)
            head_2(GROUPS - 1)
            head_y(GROUPS - 1)
            pe.wait_ge(low_maxed, 1)
            nc.tensor.matmul(low_total, low_max[:, :], ones_col[:, :], start=True, stop=True).then_inc(low_totalled, 1)
            pe.wait_ge(redo_known, 1)
            with pe.If(pe.value_load(redo[:, :], min_val=0, max_val=1) != 0):
                with pe.Fori(GROUPS, MAX_PASSES) as r:
                    transform_general(r, r - GROUPS)
                    head_1(r)
                    head_2(r)
                    head_y(r)

        @block.vector
        def _(dve):
            nc.vector.memset(ones_row[:], 1.0).then_inc(ones_set, 1)
            nc.vector.memset(l1[:], 1.0).then_inc(ones_set, 1)
            nc.vector.memset(l2[:], 1.0).then_inc(ones_set, 1)
            for c in range(CHUNKS):
                dve.wait_ge(w_landed[c], 16)
                nc.vector.tensor_tensor(w_rest[:, c], w_sb[:, c], upper(w_sb[:, c]), ALU.subtract).then_inc(w_rested, 1)
                dve.wait_ge(w_rested, c + 1)
                nc.vector.tensor_tensor(w_low[:, c], w_rest[:, c], upper(w_rest[:, c]), ALU.subtract).then_inc(w_split, 1)
            dve.wait_ge(rem_landed, 16 * 3 * PARTS)
            nc.vector.tensor_tensor(wr_rest[:], wr_sb[:], upper(wr_sb[:, :]), ALU.subtract).then_inc(wr_step, 1)
            dve.wait_ge(wr_step, 1)
            nc.vector.tensor_copy(wr_parts[0:PART], upper(wr_sb[0:PART])).then_inc(wr_step, 1)
            nc.vector.tensor_copy(wr_parts[PART:2 * PART], upper(wr_rest[PART:2 * PART])).then_inc(wr_step, 1)
            nc.vector.tensor_tensor(wr_parts[2 * PART:], wr_rest[2 * PART:], upper(wr_rest[2 * PART:]),
                                    ALU.subtract).then_inc(wr_step, 1)
            nc.vector.memset(low_sums[:, GROUPS * CHUNKS:], 0.0).then_inc(ones_set, 1)
            nc.vector.memset(ones_col[:], 1.0).then_inc(wr_step, 1)

            def mix(r, g):
                u = ut[:, 0:1, bass.ts(g, GR)].to_broadcast([P, 2, GR])
                t = ut[:, 1:2, bass.ts(g, GR)].to_broadcast([P, 2, GR])
                acc = ft[:, g].rearrange("p (s r) -> p s r", s=2)
                dve.wait_ge(ft_done, r + 1)
                nc.vector.tensor_tensor(by_us[:], acc, u, ALU.mult).then_inc(mix_step, 1)
                nc.vector.tensor_tensor(by_them[:], acc, t, ALU.mult).then_inc(mix_step, 1)
                dve.wait_ge(mix_step, 4 * r + 2)
                nc.vector.tensor_tensor(mixed[:, 0], by_us[:, 0], by_them[:, 1], ALU.add).then_inc(mix_step, 1)
                nc.vector.tensor_tensor(mixed[:, 1], by_us[:, 1], by_them[:, 0], ALU.add).then_inc(mix_step, 1)
                dve.wait_ge(mix_step, 4 * r + 4)
                nc.vector.tensor_scalar(l0[:], mixed[:], 0.0, 1.0, ALU.max, ALU.min).then_inc(l0_ready, 1)

            def clip_head(r, g):
                dve.wait_ge(h1_done, r + 1)
                nc.vector.tensor_scalar(l1[0:L2, :], h1, 0.0, 1.0, ALU.max, ALU.min).then_inc(l1_ready, 1)
                dve.wait_ge(h2_done, r + 1)
                nc.vector.tensor_scalar(l2[0:L3, :], h2, 0.0, 1.0, ALU.max, ALU.min).then_inc(l2_ready, 1)
                dve.wait_ge(hy_done, r + 1)
                nc.vector.tensor_copy(y_sb[:, bass.ts(g, GR)], hy).then_inc(y_ready, 1)

            dve.wait_ge(ones_set, 4)
            dve.wait_ge(ut_copied, 4)
            with dve.Fori(0, GROUPS) as g:
                mix(g, g)
                clip_head(g, g)

            for c in range(CHUNKS):
                dve.wait_ge(x_checked[c], GROUPS)
            dve.wait_ge(rem_checked, 1)
            nc.vector.tensor_reduce(low_max[:], low_sums[:], AX_X, ALU.max).then_inc(low_maxed, 1)
            dve.wait_ge(low_totalled, 1)
            nc.vector.tensor_scalar(redo[:], low_total, 1.0, None, ALU.min).then_inc(redo_known, 1)
            dve.wait_ge(redo_known, 1)
            dve.wait_ge(out_stored, 16)
            with dve.If(dve.value_load(redo[:, :], min_val=0, max_val=1) != 0):
                with dve.Fori(GROUPS, MAX_PASSES) as r:
                    mix(r, r - GROUPS)
                    clip_head(r, r - GROUPS)


def kernel(r_us, r_them, r_w_in, r_b_in, L0_rec_W_ft, L0_rec_b_ft, L0_rec_W1, L0_rec_b1, L0_rec_W2, L0_rec_b2,
           L0_rec_Wo, L0_rec_bo):
    import numpy as np
    import concourse.bacc as bacc
    from concourse.bass_utils import run_bass_kernel_spmd

    flat = CHUNKS * T * P
    both = np.stack([np.asarray(r_w_in), np.asarray(r_b_in)])
    w_ft = np.asarray(L0_rec_W_ft)
    main = both[:, :, :flat].reshape(2, GROUPS, GR, CHUNKS, T, P).transpose(1, 3, 5, 4, 0, 2)
    rem = both[:, :, flat:].reshape(2, GROUPS, GR, REM).transpose(3, 1, 0, 2)
    arrays = {
        "x_main": main.reshape(GROUPS, CHUNKS, P, T, GC),
        "x_rem": rem.reshape(REM, GROUPS, GC),
        "w_main": w_ft[:flat].reshape(CHUNKS, T, P, L1).transpose(0, 2, 1, 3),
        "w_rem": w_ft[flat:],
        "b_ft": np.asarray(L0_rec_b_ft).reshape(1, L1),
        "us": np.asarray(r_us).reshape(1, ROWS),
        "them": np.asarray(r_them).reshape(1, ROWS),
        "W1": np.asarray(L0_rec_W1).reshape(2, L1, L2).transpose(1, 0, 2),
        "b1": np.asarray(L0_rec_b1).reshape(1, L2),
        "W2": np.asarray(L0_rec_W2),
        "b2": np.asarray(L0_rec_b2).reshape(1, L3),
        "Wo": np.asarray(L0_rec_Wo),
        "bo": np.asarray(L0_rec_bo).reshape(1, 1),
    }
    arrays = {name: np.ascontiguousarray(a) for name, a in arrays.items()}
    nc = bacc.Bacc("TRN2", target_bir_lowering=False, num_devices=1)
    args = [nc.dram_tensor(name, a.shape, mybir.dt.from_np(a.dtype), kind="ExternalInput").ap()
            for name, a in arrays.items()]
    out = nc.dram_tensor("out", (1, ROWS), F32, kind="ExternalOutput").ap()
    build(nc, *args, out)
    got = run_bass_kernel_spmd(nc, [arrays], core_ids=[0]).results[0]["out"]
    return got.reshape(ROWS, 1)
```

```python
from contextlib import ExitStack

import concourse.bass as bass
from concourse import mybir

F32 = mybir.dt.float32
F32R = mybir.dt.float32r
BF16 = mybir.dt.bfloat16
U16 = mybir.dt.uint16
U32 = mybir.dt.uint32
I32 = mybir.dt.int32
ALU = mybir.AluOpType
ACT = mybir.ActivationFunctionType
AX_X = mybir.AxisListType.X

P = 128
ROWS = 1024
FEATS = 5128
L1, L2, L3 = 128, 32, 32
ROUNDS = 4
GR = ROWS // ROUNDS
GC = 2 * GR
T = 4
SLOTS = FEATS // (P * T)
TILES = SLOTS * T
REM = FEATS - TILES * P
FULL = ROUNDS - 1
HALVES = 2
HR, HC, HT = GR // HALVES, GC // HALVES, T * HALVES
HSLOTS = SLOTS // HALVES
CUTS = (0, 2, 4, 6, 7, 8)
PIECES = len(CUTS) - 1
assert CUTS[-1] == HT


def pieces(c):
    cuts = CUTS if c == SLOTS - 1 else (0, HT // 2, HT)
    return [(k, cuts[k], cuts[k + 1]) for k in range(len(cuts) - 1)]


GROUPS = FULL + HALVES
PART = 32
PARTS = 2
HIGH_BITS = 0xFFFFF000
UT = 2
UNIT = UT * GC
UNITS = TILES // UT
BUFFERS = 4
STREAMING, GENERAL = 0, 1
Q = P // L2
QR = ROWS // Q
REM_LOADS = 16 * (1 + 2 * PARTS)
HEAD_LOADS = 16 * (1 + 2 * Q + 3)
SPLIT_REM_AT, ADD_REM_AT = 5, 7
LOW_SUMS = ROUNDS * SLOTS + PIECES


def lower(ap):
    return ap.bitcast(U16)[..., 0::2]


def build(nc, x_main, x_last, x_rem, w_main, w_rem, b_ft, us, them, W1, b1, W2, b2, Wo, bo, out):
    with ExitStack() as ctx:
        def sb(name, shape, dt=F32):
            return ctx.enter_context(nc.sbuf_tensor(name, shape, dt))

        def sem(name):
            return ctx.enter_context(nc.semaphore(name))

        x_ring = sb("x_ring", [P, SLOTS, T * GC])
        x_full = x_ring[:, :, :].rearrange("p s (t n) -> p s t n", t=T)
        x_half = x_ring[:, :, :].rearrange("p s (t n) -> p s t n", t=HT)
        w_sb = sb("w_sb", [P, TILES, L1])
        w_cut = sb("w_cut", [P, 2, T * L1])
        w_high = sb("w_high", [P, TILES, L1], F32R)
        w_low = sb("w_low", [P, TILES, L1], F32R)
        x_unit = sb("x_unit", [P, BUFFERS, UNIT], F32R)
        xr_sb = sb("xr_sb", [PARTS * PART, ROUNDS * GC])
        wr_sb = sb("wr_sb", [PARTS * PART, L1])
        xr_unit = sb("xr_unit", [PARTS * PART, ROUNDS * GC], F32R)
        wr_cut = sb("wr_cut", [PARTS * PART, L1])
        wr_parts = sb("wr_parts", [PARTS * PART, L1], F32R)
        low_sums = sb("low_sums", [P, LOW_SUMS])
        low_copy = sb("low_copy", [P, 2, T * GC], BF16)
        low_max = sb("low_max", [P, 1])
        ones_col = sb("ones_col", [P, 1])
        redo = sb("redo", [1, 1], I32)
        ones_row = sb("ones_row", [1, GR])
        ut = sb("ut", [P, 2, ROWS])
        w1_sb = sb("w1_sb", [P, 2, L2])
        w2_sb = sb("w2_sb", [P, Q * L3])
        wo_sb = sb("wo_sb", [P, Q])
        b1_sb = sb("b1_sb", [1, Q, L2])
        b2_sb = sb("b2_sb", [1, Q, L3])
        bo_sb = sb("bo_sb", [1, Q, 1])
        by_them = sb("by_them", [P, 2, GR])
        mixed = sb("mixed", [P, 2, GR])
        l0 = sb("l0", [P, 2, GR])
        l1 = sb("l1", [P, GR // Q])
        l2 = sb("l2", [P, GR // Q])
        y_sb = sb("y_sb", [Q, QR])

        ft = ctx.enter_context(nc.psum_tensor("ft", [P, ROUNDS, GC], F32))
        bc = ctx.enter_context(nc.psum_tensor("bc", [P, 4, 512], F32))
        by_us = bc[:, 3, 0:GC].rearrange("p (s r) -> p s r", s=2)
        low_total = ft[0:1, 1, 0:1]

        def head_psum(i, n):
            return bc[0:Q if i == 2 else P, i, 0:n // Q]

        x_landed = [sem(f"x_landed{c}") for c in range(SLOTS)]
        piece_landed = [[sem(f"piece_landed{c}_{k}") for k, _, _ in pieces(c)] for c in range(SLOTS)]
        slot_used = [sem(f"slot_used{c}") for c in range(SLOTS)]
        slot_checked = [sem(f"slot_checked{c}") for c in range(SLOTS)]
        w_landed = [sem(f"w_landed{c}") for c in range(SLOTS)]
        piece_checked = sem("piece_checked")
        rem_checked = sem("rem_checked")
        converted = sem("converted")
        unit_used = sem("unit_used")
        w_masked = sem("w_masked")
        w_split = sem("w_split")
        wr_step = sem("wr_step")
        filled = sem("filled")
        rem_landed = sem("rem_landed")
        rem_copied = sem("rem_copied")
        ut_landed = sem("ut_landed")
        head_landed = sem("head_landed")
        ones_set = sem("ones_set")
        ut_spread = sem("ut_spread")
        ut_copied = sem("ut_copied")
        mix_step = sem("mix_step")
        l0_ready = sem("l0_ready")
        h1_done = sem("h1_done")
        l1_ready = sem("l1_ready")
        h2_done = sem("h2_done")
        l2_ready = sem("l2_ready")
        hy_done = sem("hy_done")
        y_ready = sem("y_ready")
        out_stored = sem("out_stored")
        low_maxed = sem("low_maxed")
        general_done = sem("general_done")
        low_totalled = sem("low_totalled")
        redo_known = sem("redo_known")

        def half_bank(h):
            return ft[:, (FULL + h) % ROUNDS, 0:HC]

        block = ctx.enter_context(nc.Block())

        @block.sync
        def _(sp):
            def slot_free(r, c):
                sp.wait_ge(converted, UNITS * (r - 1) + T // UT * (c + 1))
                sp.wait_ge(slot_checked[c], r)

            def load_last_round(r, path):
                for c in range(SLOTS):
                    if path == STREAMING:
                        slot_free(r, c)
                    else:
                        sp.wait_ge(slot_used[c], FULL)
                    for k, a, b in pieces(c):
                        sp.dma_start(x_half[:, c, a:b], x_last[c, :, a:b]).then_inc(piece_landed[c][k], 16)

            for c in range(SLOTS):
                sp.dma_start(w_sb[:, T * c:T * c + T], w_main[c]).then_inc(w_landed[c], 16)
                sp.dma_start(x_full[:, c], x_main[0, c]).then_inc(x_landed[c], 16)
            with sp.Fori(1, FULL) as r:
                for c in range(SLOTS):
                    slot_free(r, c)
                    sp.dma_start(x_full[:, c], x_main[r, c]).then_inc(x_landed[c], 16)
            load_last_round(FULL, STREAMING)
            sp.wait_ge(y_ready, GROUPS)
            sp.dma_start(out, y_sb[:, :]).then_inc(out_stored, 16)
            sp.wait_ge(redo_known, 1)
            general = sp.value_load(redo[:, :], min_val=0, max_val=1)
            sp.wait_ge(out_stored, 16)
            with sp.If(general != 0):
                for c in range(SLOTS):
                    sp.dma_start(x_full[:, c], x_main[0, c]).then_inc(x_landed[c], 16)
                with sp.Fori(1, FULL) as r:
                    for c in range(SLOTS):
                        sp.wait_ge(slot_used[c], r)
                        sp.dma_start(x_full[:, c], x_main[r, c]).then_inc(x_landed[c], 16)
                load_last_round(FULL, GENERAL)
                sp.wait_ge(y_ready, 2 * GROUPS)
                sp.dma_start(out, y_sb[:, :]).then_inc(out_stored, 16)
                sp.wait_ge(out_stored, 32)

        @block.gpsimd
        def _(pool):
            nc.gpsimd.memset(xr_sb[:], 1.0).then_inc(filled, 1)
            nc.gpsimd.memset(wr_sb[:], 0.0).then_inc(filled, 1)
            nc.gpsimd.memset(w2_sb[:], 0.0).then_inc(filled, 1)
            nc.gpsimd.memset(wo_sb[:], 0.0).then_inc(filled, 1)

        @block.scalar
        def _(act):
            act.dma_start(ut[0:1, 0], us).then_inc(ut_landed, 16)
            act.dma_start(ut[0:1, 1], them).then_inc(ut_landed, 16)
            act.wait_ge(filled, 4)
            act.dma_start(xr_sb[0:REM, :], x_rem).then_inc(rem_landed, 16)
            for k in range(0, PARTS * PART, PART):
                act.dma_start(wr_sb[k:k + REM, :], w_rem).then_inc(rem_landed, 16)
                act.dma_start(wr_sb[k + REM:k + REM + 1, :], b_ft).then_inc(rem_landed, 16)
            act.wait_ge(rem_landed, REM_LOADS)
            for k in range(PART, PARTS * PART, PART):
                nc.scalar.copy(xr_sb[k:k + REM, :], xr_sb[0:REM, :]).then_inc(rem_copied, 1)
            act.dma_start(w1_sb[:], W1).then_inc(head_landed, 16)
            for q in range(Q):
                act.dma_start(w2_sb[L2 * q:L2 * q + L2, L3 * q:L3 * q + L3], W2).then_inc(head_landed, 16)
                act.dma_start(wo_sb[L3 * q:L3 * q + L3, q:q + 1], Wo).then_inc(head_landed, 16)
            for dst, src in ((b1_sb, b1), (b2_sb, b2), (bo_sb, bo)):
                act.dma_start(dst[:], src.to_broadcast(dst.shape)).then_inc(head_landed, 16)
            for h in range(4):
                act.wait_ge(ut_spread, h + 1)
                nc.scalar.copy(ut[:, h // 2, 512 * (h % 2):512 * (h % 2) + 512], bc[:, h]).then_inc(ut_copied, 1)

            def sum_low(r, c, loads, first=False):
                for landed, count in loads:
                    act.wait_ge(landed, count)
                if c >= 2:
                    act.wait_ge(slot_checked[c - 2], r + 1)
                elif not first:
                    act.wait_ge(slot_checked[c - 2], r)
                nc.scalar.activation(low_copy[:, c % 2], lower(x_ring[:, c]), ACT.Copy,
                                     accum_out=low_sums[:, bass.ds(r * SLOTS + c, 1)]).then_inc(slot_checked[c], 1)

            for c in range(SLOTS):
                sum_low(0, c, [(x_landed[c], 16)], first=True)
            act.wait_ge(ones_set, 2)
            act.wait_ge(slot_checked[SLOTS - 2], 1)
            nc.scalar.activation(low_copy[0:REM, 0], lower(xr_sb[0:REM, :]), ACT.Copy,
                                 accum_out=low_sums[0:REM, LOW_SUMS - 1:]).then_inc(rem_checked, 1)
            act.wait_ge(rem_checked, 1)
            with act.Fori(1, FULL) as r:
                for c in range(SLOTS):
                    sum_low(r, c, [(x_landed[c], 16 * (r + 1))])
            for c in range(SLOTS - 1):
                sum_low(FULL, c, [(landed, 16) for landed in piece_landed[c]])
            for k, a, b in pieces(SLOTS - 1):
                act.wait_ge(piece_landed[SLOTS - 1][k], 16)
                if k >= 2:
                    act.wait_ge(piece_checked, k - 1)
                else:
                    act.wait_ge(slot_checked[SLOTS - 3 + k], ROUNDS)
                nc.scalar.activation(low_copy[:, (SLOTS - 1 + k) % 2, 0:HC * (b - a)],
                                     lower(x_ring[:, SLOTS - 1, HC * a:HC * b]), ACT.Copy,
                                     accum_out=low_sums[:, FULL * SLOTS + SLOTS - 1 + k:FULL * SLOTS + SLOTS + k]
                                     ).then_inc(piece_checked, 1)

        @block.tensor
        def _(pe):
            def add_unit(bank, n, buf, w0, tiles, cols, start=False, stop=False):
                x = x_unit[:, buf, 0:tiles * cols].rearrange("p (t n) -> p t n", t=tiles)
                pe.wait_ge(converted, n + 1)
                for t in range(tiles):
                    nc.tensor.matmul(bank, w_high[:, w0 + t], x[:, t], start=start and t == 0, stop=False)
                    mm = nc.tensor.matmul(bank, w_low[:, w0 + t], x[:, t], start=False,
                                          stop=stop and t == tiles - 1)
                mm.then_inc(unit_used, 1)

            def add_whole(bank, x, n, w0, start):
                for t in range(n):
                    mm = nc.tensor.matmul(bank, w_sb[:, w0 + t], x[:, t], start=start and t == 0, stop=False)
                return mm

            def add_rem(bank, col, n, path):
                if path == STREAMING:
                    return nc.tensor.matmul(bank, wr_parts[:, :], xr_unit[:, bass.ds(col, n)], start=False, stop=False)
                return nc.tensor.matmul(bank, wr_sb[0:PART, :], xr_sb[0:PART, bass.ds(col, n)], start=False, stop=True)

            def head_step(i, s, n):
                m = n // Q
                sums = head_psum(i, n)
                bias = (b1_sb, b2_sb, bo_sb)[i][:, :, :].rearrange("a q m -> a (q m)")
                nc.tensor.matmul(sums, bias, ones_row[:, 0:m], start=True, stop=False)
                if i == 0:
                    pe.wait_ge(l0_ready, s + 1)
                    for q in range(Q):
                        for side in range(2):
                            mm = nc.tensor.matmul(sums[L2 * q:L2 * q + L2], w1_sb[:, side],
                                                  l0[:, side, m * q:m * q + m], start=False, stop=side == 1)
                    mm.then_inc(h1_done, 1)
                if i == 1:
                    pe.wait_ge(l1_ready, s + 1)
                    nc.tensor.matmul(sums, w2_sb[:, :], l1[:, 0:m], start=False, stop=True).then_inc(h2_done, 1)
                if i == 2:
                    pe.wait_ge(l2_ready, s + 1)
                    nc.tensor.matmul(sums, wo_sb[:, :], l2[:, 0:m], start=False, stop=True).then_inc(hy_done, 1)

            def full_group(r, before, first=False):
                for c in range(SLOTS):
                    if first:
                        pe.wait_ge(w_split, 2 * c + 2)
                    for u in range(T // UT * c, T // UT * (c + 1)):
                        add_unit(ft[:, r], UNITS * r + u, u % BUFFERS, UT * u, UT, GC, u == 0, u == UNITS - 1)
                    if first and c == 0:
                        pe.wait_ge(ones_set, 1)
                        pe.wait_ge(ut_landed, 32)
                        for h in range(4):
                            nc.tensor.matmul(bc[:, h], ones_row[:, 0:P],
                                             ut[0:1, h // 2, 512 * (h % 2):512 * (h % 2) + 512],
                                             start=True, stop=True).then_inc(ut_spread, 1)
                    if c == (ADD_REM_AT if first else 1):
                        if first:
                            pe.wait_ge(wr_step, 4)
                        add_rem(ft[:, r], r * GC, GC, STREAMING)
                    if before is not None and 2 <= c < 5:
                        head_step(c - 2, before, GR)

            def half_group(h, before, rows_before):
                bank, col = half_bank(h), FULL * GC + h * HC
                for i in range(HSLOTS):
                    c = h * HSLOTS + i
                    for k, a, b in pieces(c):
                        u = T // UT * c + k
                        add_unit(bank, UNITS * FULL + u, u % BUFFERS, HT * i + a, b - a, HC, i == 0 and a == 0,
                                 i == HSLOTS - 1 and b == HT)
                    if i == 1:
                        add_rem(bank, col, HC, STREAMING)
                    if 1 <= i < 4:
                        head_step(i - 1, before, rows_before)

            def full_group_general(g):
                for c in range(SLOTS):
                    pe.wait_ge(x_landed[c], 16 * (g + FULL + 1))
                    add_whole(ft[:, g], x_full[:, c], T, T * c, c == 0).then_inc(slot_used[c], 1)
                add_rem(ft[:, g], g * GC, GC, GENERAL).then_inc(general_done, 1)

            def half_group_general(h):
                for i in range(HSLOTS):
                    c = h * HSLOTS + i
                    for k, a, b in pieces(c):
                        pe.wait_ge(piece_landed[c][k], 32)
                        mm = add_whole(half_bank(h), x_half[:, c, a:b], b - a, HT * i + a, i == 0 and a == 0)
                    mm.then_inc(slot_used[c], 1)
                add_rem(half_bank(h), FULL * GC + h * HC, HC, GENERAL).then_inc(general_done, 1)

            full_group(0, None, first=True)
            pe.wait_ge(head_landed, HEAD_LOADS)
            pe.wait_ge(ut_copied, 4)
            with pe.Fori(1, FULL) as g:
                full_group(g, g - 1)
            half_group(0, FULL - 1, GR)
            half_group(1, FULL, HR)
            head_step(0, GROUPS - 1, HR)
            pe.wait_ge(low_maxed, 1)
            nc.tensor.matmul(low_total, low_max[:, :], ones_col[:, :], start=True, stop=True).then_inc(low_totalled, 1)
            head_step(1, GROUPS - 1, HR)
            head_step(2, GROUPS - 1, HR)

            pe.wait_ge(redo_known, 1)
            with pe.If(pe.value_load(redo[:, :], min_val=0, max_val=1) != 0):
                with pe.Fori(0, FULL) as g:
                    full_group_general(g)
                    for i in range(3):
                        head_step(i, g + GROUPS, GR)
                for h in range(HALVES):
                    half_group_general(h)
                    for i in range(3):
                        head_step(i, GROUPS + FULL + h, HR)

        @block.vector
        def _(dve):
            nc.vector.memset(ones_row[:], 1.0).then_inc(ones_set, 1)
            nc.vector.memset(low_sums[:, LOW_SUMS - 1:], 0.0).then_inc(ones_set, 1)
            nc.vector.memset(ones_col[:], 1.0).then_inc(ones_set, 1)

            def split_weights(c):
                w = w_sb[:, T * c:T * c + T].rearrange("p t m -> p (t m)")
                high = w_high[:, T * c:T * c + T].rearrange("p t m -> p (t m)")
                low = w_low[:, T * c:T * c + T].rearrange("p t m -> p (t m)")
                dve.wait_ge(w_landed[c], 16)
                nc.vector.tensor_scalar(w_cut[:, c % 2].bitcast(U32), w.bitcast(U32), HIGH_BITS, None,
                                        ALU.bitwise_and).then_inc(w_masked, 1)
                dve.wait_ge(w_masked, c + 1)
                nc.vector.tensor_copy(high, w_cut[:, c % 2]).then_inc(w_split, 1)
                nc.vector.tensor_tensor(low, w, w_cut[:, c % 2], ALU.subtract).then_inc(w_split, 1)

            def split_rem():
                dve.wait_ge(rem_landed, REM_LOADS)
                nc.vector.tensor_scalar(wr_cut[:].bitcast(U32), wr_sb[:].bitcast(U32), HIGH_BITS, None,
                                        ALU.bitwise_and).then_inc(wr_step, 1)
                dve.wait_ge(wr_step, 1)
                nc.vector.tensor_copy(wr_parts[0:PART], wr_cut[0:PART]).then_inc(wr_step, 1)
                nc.vector.tensor_tensor(wr_parts[PART:], wr_sb[PART:], wr_cut[PART:], ALU.subtract).then_inc(wr_step, 1)
                dve.wait_ge(rem_copied, PARTS - 1)
                nc.vector.tensor_copy(xr_unit[:], xr_sb[:]).then_inc(wr_step, 1)

            def convert(n, buf, x, wait):
                if wait:
                    dve.wait_ge(unit_used, n + 1 - BUFFERS)
                nc.vector.tensor_copy(x_unit[:, buf, 0:x.shape[-1]], x).then_inc(converted, 1)

            def convert_slot(r, c, first=False):
                dve.wait_ge(x_landed[c], 16 * (r + 1))
                for k in range(T // UT):
                    u = T // UT * c + k
                    convert(UNITS * r + u, u % BUFFERS, x_ring[:, c, UNIT * k:UNIT * (k + 1)],
                            not first or u >= BUFFERS)

            def mix(s, bank, row, n):
                u = ut[:, 0:1, bass.ds(row, n)].to_broadcast([P, 2, n])
                t = ut[:, 1:2, bass.ds(row, n)].to_broadcast([P, 2, n])
                acc = bank.rearrange("p (s r) -> p s r", s=2)
                nc.vector.tensor_tensor(by_us[:, :, 0:n], acc, u, ALU.mult).then_inc(mix_step, 1)
                nc.vector.tensor_tensor(by_them[:, :, 0:n], acc, t, ALU.mult).then_inc(mix_step, 1)
                dve.wait_ge(mix_step, 3 * s + 2)
                nc.vector.tensor_tensor(mixed[:, :, 0:n], by_us[:, :, 0:n], by_them[:, ::-1, 0:n],
                                        ALU.add).then_inc(mix_step, 1)
                dve.wait_ge(mix_step, 3 * s + 3)
                nc.vector.tensor_scalar(l0[:, :, 0:n], mixed[:, :, 0:n], 0.0, 1.0, ALU.max,
                                        ALU.min).then_inc(l0_ready, 1)

            def clip_l1(s, n):
                dve.wait_ge(h1_done, s + 1)
                nc.vector.tensor_scalar(l1[:, 0:n // Q], head_psum(0, n), 0.0, 1.0, ALU.max,
                                        ALU.min).then_inc(l1_ready, 1)

            def clip_l2(s, n):
                dve.wait_ge(h2_done, s + 1)
                nc.vector.tensor_scalar(l2[:, 0:n // Q], head_psum(1, n), 0.0, 1.0, ALU.max,
                                        ALU.min).then_inc(l2_ready, 1)

            def copy_y(s, col, n):
                dve.wait_ge(hy_done, s + 1)
                nc.vector.tensor_copy(y_sb[:, bass.ds(col, n // Q)], head_psum(2, n)).then_inc(y_ready, 1)

            for c in range(SLOTS):
                split_weights(c)
                convert_slot(0, c, first=True)
                if c == SPLIT_REM_AT:
                    split_rem()
            dve.wait_ge(ut_copied, 4)
            with dve.Fori(1, FULL) as r:
                for c in range(SLOTS):
                    convert_slot(r, c)
                    if c == 1:
                        dve.wait_ge(unit_used, UNITS * r)
                        mix(r - 1, ft[:, r - 1], (r - 1) * GR, GR)
                    if c == 3:
                        clip_l1(r - 1, GR)
                    if c == 4:
                        clip_l2(r - 1, GR)
                    if c == 5:
                        copy_y(r - 1, (r - 1) * (GR // Q), GR)
            before = (FULL - 1, ft[:, FULL - 1], (FULL - 1) * GR, GR)
            used = UNITS * FULL
            for h in range(HALVES):
                s, bank, row, n = before
                for i in range(HSLOTS):
                    c = h * HSLOTS + i
                    for k, a, b in pieces(c):
                        u = T // UT * c + k
                        dve.wait_ge(piece_landed[c][k], 16)
                        convert(UNITS * FULL + u, u % BUFFERS, x_ring[:, c, HC * a:HC * b], True)
                    if i == 0:
                        dve.wait_ge(unit_used, used)
                        mix(s, bank, row, n)
                    if i == 2:
                        clip_l1(s, n)
                    if i == 3:
                        clip_l2(s, n)
                    if i == 4:
                        copy_y(s, row // Q, n)
                used += sum(len(pieces(h * HSLOTS + i)) for i in range(HSLOTS))
                before = (FULL + h, half_bank(h), FULL * GR + h * HR, HR)
            s, bank, row, n = before
            dve.wait_ge(unit_used, used)
            mix(s, bank, row, n)
            for c in range(SLOTS - 1):
                dve.wait_ge(slot_checked[c], ROUNDS)
            dve.wait_ge(slot_checked[SLOTS - 1], FULL)
            dve.wait_ge(piece_checked, PIECES)
            dve.wait_ge(rem_checked, 1)
            nc.vector.tensor_reduce(low_max[:], low_sums[:], AX_X, ALU.max).then_inc(low_maxed, 1)
            clip_l1(s, n)
            dve.wait_ge(low_totalled, 1)
            nc.vector.tensor_scalar(redo[:], low_total, 1.0, None, ALU.min).then_inc(redo_known, 1)
            clip_l2(s, n)
            copy_y(s, row // Q, n)

            dve.wait_ge(redo_known, 1)
            general = dve.value_load(redo[:, :], min_val=0, max_val=1)
            with dve.If(general != 0):
                dve.wait_ge(out_stored, 16)
                with dve.Fori(0, FULL) as g:
                    dve.wait_ge(general_done, g + 1)
                    mix(g + GROUPS, ft[:, g], g * GR, GR)
                    clip_l1(g + GROUPS, GR)
                    clip_l2(g + GROUPS, GR)
                    copy_y(g + GROUPS, g * (GR // Q), GR)
                for h in range(HALVES):
                    s, row = GROUPS + FULL + h, FULL * GR + h * HR
                    dve.wait_ge(general_done, FULL + h + 1)
                    mix(s, half_bank(h), row, HR)
                    clip_l1(s, HR)
                    clip_l2(s, HR)
                    copy_y(s, row // Q, HR)


def kernel(r_us, r_them, r_w_in, r_b_in, L0_rec_W_ft, L0_rec_b_ft, L0_rec_W1, L0_rec_b1, L0_rec_W2, L0_rec_b2,
           L0_rec_Wo, L0_rec_bo):
    import numpy as np
    import concourse.bacc as bacc
    from concourse.bass_utils import run_bass_kernel_spmd

    flat, split = TILES * P, FULL * GR
    cuts = [g * GR // Q for g in range(FULL)] + [(split + h * HR) // Q for h in range(HALVES)] + [QR]
    quarters = np.arange(ROWS).reshape(Q, QR)
    order = np.concatenate([quarters[:, a:b].reshape(-1) for a, b in zip(cuts, cuts[1:])])
    both = np.stack([np.asarray(r_w_in)[order], np.asarray(r_b_in)[order]])
    w_ft = np.asarray(L0_rec_W_ft)
    main = both[:, :split, :flat].reshape(2, FULL, GR, SLOTS, T, P).transpose(1, 3, 5, 4, 0, 2)
    last = both[:, split:, :flat].reshape(2, HALVES, HR, HSLOTS, HT, P).transpose(1, 3, 5, 4, 0, 2)
    rem = both[:, :, flat:].transpose(2, 0, 1)
    rem = [rem[:, :, g * GR:(g + 1) * GR] for g in range(FULL)] + \
          [rem[:, :, split + h * HR:split + (h + 1) * HR] for h in range(HALVES)]
    arrays = {
        "x_main": main.reshape(FULL, SLOTS, P, T, GC),
        "x_last": last.reshape(SLOTS, P, HT, HC),
        "x_rem": np.concatenate([part.reshape(REM, -1) for part in rem], axis=1),
        "w_main": w_ft[:flat].reshape(SLOTS, T, P, L1).transpose(0, 2, 1, 3),
        "w_rem": w_ft[flat:],
        "b_ft": np.asarray(L0_rec_b_ft).reshape(1, L1),
        "us": np.asarray(r_us)[order].reshape(1, ROWS),
        "them": np.asarray(r_them)[order].reshape(1, ROWS),
        "W1": np.asarray(L0_rec_W1).reshape(2, L1, L2).transpose(1, 0, 2),
        "b1": np.asarray(L0_rec_b1).reshape(1, 1, L2),
        "W2": np.asarray(L0_rec_W2),
        "b2": np.asarray(L0_rec_b2).reshape(1, 1, L3),
        "Wo": np.asarray(L0_rec_Wo),
        "bo": np.asarray(L0_rec_bo).reshape(1, 1, 1),
    }
    arrays = {name: np.ascontiguousarray(a) for name, a in arrays.items()}
    nc = bacc.Bacc("TRN2", target_bir_lowering=False, num_devices=1)
    args = [nc.dram_tensor(name, a.shape, mybir.dt.from_np(a.dtype), kind="ExternalInput").ap()
            for name, a in arrays.items()]
    out = nc.dram_tensor("out", (Q, QR), F32, kind="ExternalOutput").ap()
    build(nc, *args, out)
    got = run_bass_kernel_spmd(nc, [arrays], core_ids=[0]).results[0]["out"]
    return got.reshape(ROWS, 1)
```
